# Optimizing a Trainium2 kernel written in Bass

```python
import numpy as np
import jax
import jax.numpy as jnp

def _softmax(x, axis=-1):
    return jax.nn.softmax(x, axis=axis)

def _gelu(x):
    return jax.nn.gelu(x, approximate=True)

def _silu(x):
    return jax.nn.silu(x)

def _sigmoid(x):
    return jax.nn.sigmoid(x)

def _layernorm(x, axis=-1, eps=1e-05):
    m = jnp.mean(x, axis=axis, keepdims=True)
    v = jnp.var(x, axis=axis, keepdims=True)
    return (x - m) / jnp.sqrt(v + eps)

def _scatter_add(tgt, idx, src, axis=0):
    return tgt.at[idx].add(src)

def _segment_sum(src, seg, n):
    return jax.ops.segment_sum(src, seg, n)
kernel_name = 'mk_gnn_resnorm_d2_gnn_r32_6052f0'

def setup_inputs(seed: int=0):
    np.random.seed(seed)
    _w = jnp.asarray

    def _rec_inputs():
        import jax
        import jax.numpy as jnp
        _gk = jax.random.key(seed)
        x = -0.0006008 + 1.001 * jax.random.normal(jax.random.fold_in(_gk, 1), (3125, 128), jnp.float32)
        _s = jax.random.randint(jax.random.fold_in(_gk, 2), (50000,), 0, 3125, jnp.int32)
        _d = jax.random.randint(jax.random.fold_in(_gk, 3), (50000,), 0, 3125, jnp.int32)
        _loop = jnp.arange(3125, dtype=jnp.int32)
        src = jnp.concatenate([_s, _d, _loop])
        dst = jnp.concatenate([_d, _s, _loop])
        _o = jnp.argsort(dst, stable=True)
        src = src[_o]
        dst = dst[_o]
        edge_attr_20 = jax.random.uniform(jax.random.fold_in(_gk, 12), (103125, 20), jnp.float32, 0.0, 1)
        edge_weight = jax.random.uniform(jax.random.fold_in(_gk, 14), (103125,), jnp.float32, 0.0, 0.999998)
        return (x, src, dst, edge_attr_20, edge_weight)
    x, src, dst, edge_attr_20, edge_weight = _rec_inputs()

    def _L0_gnn_setup():
        import jax, jax.numpy as jnp
        import numpy as np
        N_ATOMS = 625
        N_PAIRS = 20000
        N_BASIS = 128
        N_FILTERS = 128
        N_RBF = 20

        def ssp(v):
            return jax.nn.softplus(v) - jnp.log(2.0)
        key = jax.random.key(seed)
        ks = jax.random.split(key, 16)
        s = 0.05
        return {'x': jax.random.normal(ks[0], (N_ATOMS, N_BASIS), dtype=jnp.float32), 'f_ij': jax.random.uniform(ks[1], (N_PAIRS, N_RBF), dtype=jnp.float32), 'rcut_ij': jax.random.uniform(ks[2], (N_PAIRS,), dtype=jnp.float32), 'idx_i': jax.random.randint(ks[3], (N_PAIRS,), 0, N_ATOMS), 'idx_j': jax.random.randint(ks[4], (N_PAIRS,), 0, N_ATOMS), 'W_in': jax.random.normal(ks[5], (N_BASIS, N_FILTERS), dtype=jnp.float32) * s, 'b_in': jnp.zeros((N_FILTERS,), dtype=jnp.float32), 'Wf1': jax.random.normal(ks[6], (N_RBF, N_FILTERS), dtype=jnp.float32) * s, 'bf1': jnp.zeros((N_FILTERS,), dtype=jnp.float32), 'Wf2': jax.random.normal(ks[7], (N_FILTERS, N_FILTERS), dtype=jnp.float32) * s, 'bf2': jnp.zeros((N_FILTERS,), dtype=jnp.float32), 'Wo1': jax.random.normal(ks[8], (N_FILTERS, N_BASIS), dtype=jnp.float32) * s, 'bo1': jnp.zeros((N_BASIS,), dtype=jnp.float32), 'Wo2': jax.random.normal(ks[9], (N_BASIS, N_BASIS), dtype=jnp.float32) * s, 'bo2': jnp.zeros((N_BASIS,), dtype=jnp.float32)}
    _L0_gnn_all = _L0_gnn_setup()
    _L0_gnn_in = {k: v for k, v in _L0_gnn_all.items() if k in ('W_in', 'b_in', 'Wf1', 'bf1', 'Wf2', 'bf2', 'Wo1', 'bo1', 'Wo2', 'bo2')}
    del _L0_gnn_all

    def _L1_gnn_setup():
        import jax, jax.numpy as jnp
        import numpy as np
        N_NODES = 50000
        N_EDGES = 50000
        DIM = 128
        SLOPE = 0.2
        key = jax.random.key(seed)
        ks = jax.random.split(key, 9)
        indices = jax.random.randint(ks[0], (2, N_EDGES), 0, N_NODES)
        features = jax.random.normal(ks[1], (N_NODES, DIM), dtype=jnp.float32)
        W1_w = jax.random.normal(ks[2], (DIM, DIM), dtype=jnp.float32) * 0.05
        W1_b = jax.random.normal(ks[3], (DIM,), dtype=jnp.float32) * 0.05
        W2_w = jax.random.normal(ks[4], (DIM, DIM), dtype=jnp.float32) * 0.05
        W2_b = jax.random.normal(ks[5], (DIM,), dtype=jnp.float32) * 0.05
        Watt_w = jax.random.normal(ks[6], (DIM, DIM), dtype=jnp.float32) * 0.05
        Watt_b = jax.random.normal(ks[7], (DIM,), dtype=jnp.float32) * 0.05
        a = jax.random.normal(ks[8], (2 * DIM, 1), dtype=jnp.float32) * 0.05
        return {'indices': indices, 'features': features, 'num_nodes': N_NODES, 'W1_w': W1_w, 'W1_b': W1_b, 'W2_w': W2_w, 'W2_b': W2_b, 'Watt_w': Watt_w, 'Watt_b': Watt_b, 'a': a}
    _L1_gnn_all = _L1_gnn_setup()
    _L1_gnn_in = {k: v for k, v in _L1_gnn_all.items() if k in ('W1_w', 'W1_b', 'W2_w', 'W2_b', 'Watt_w', 'Watt_b', 'a')}
    del _L1_gnn_all
    return {'x': x, 'src': src, 'dst': dst, 'edge_attr_20': edge_attr_20, 'edge_weight': edge_weight, 'L0_gnn_W_in': _L0_gnn_in['W_in'], 'L0_gnn_b_in': _L0_gnn_in['b_in'], 'L0_gnn_Wf1': _L0_gnn_in['Wf1'], 'L0_gnn_bf1': _L0_gnn_in['bf1'], 'L0_gnn_Wf2': _L0_gnn_in['Wf2'], 'L0_gnn_bf2': _L0_gnn_in['bf2'], 'L0_gnn_Wo1': _L0_gnn_in['Wo1'], 'L0_gnn_bo1': _L0_gnn_in['bo1'], 'L0_gnn_Wo2': _L0_gnn_in['Wo2'], 'L0_gnn_bo2': _L0_gnn_in['bo2'], 'L1_gnn_W1_w': _L1_gnn_in['W1_w'], 'L1_gnn_W1_b': _L1_gnn_in['W1_b'], 'L1_gnn_W2_w': _L1_gnn_in['W2_w'], 'L1_gnn_W2_b': _L1_gnn_in['W2_b'], 'L1_gnn_Watt_w': _L1_gnn_in['Watt_w'], 'L1_gnn_Watt_b': _L1_gnn_in['Watt_b'], 'L1_gnn_a': _L1_gnn_in['a']}

def reference(x, src, dst, edge_attr_20, edge_weight, L0_gnn_W_in, L0_gnn_b_in, L0_gnn_Wf1, L0_gnn_bf1, L0_gnn_Wf2, L0_gnn_bf2, L0_gnn_Wo1, L0_gnn_bo1, L0_gnn_Wo2, L0_gnn_bo2, L1_gnn_W1_w, L1_gnn_W1_b, L1_gnn_W2_w, L1_gnn_W2_b, L1_gnn_Watt_w, L1_gnn_Watt_b, L1_gnn_a):
    import jax
    import jax.numpy as jnp

    def _L0_gnn_ref(x, f_ij, rcut_ij, idx_i, idx_j, W_in, b_in, Wf1, bf1, Wf2, bf2, Wo1, bo1, Wo2, bo2):
        import jax, jax.numpy as jnp
        import numpy as np
        N_ATOMS = 625
        N_PAIRS = 20000
        N_BASIS = 128
        N_FILTERS = 128
        N_RBF = 20

        def ssp(v):
            return jax.nn.softplus(v) - jnp.log(2.0)
        n_atoms = x.shape[0]
        h = x @ W_in + b_in
        Wij = ssp(f_ij @ Wf1 + bf1) @ Wf2 + bf2
        Wij = Wij * rcut_ij[:, None]
        x_ij = h[idx_j] * Wij
        agg = jax.ops.segment_sum(x_ij, idx_i, num_segments=n_atoms)
        out = ssp(agg @ Wo1 + bo1) @ Wo2 + bo2
        return out

    def _L1_gnn_ref(indices, features, num_nodes, W1_w, W1_b, W2_w, W2_b, Watt_w, Watt_b, a):
        import jax, jax.numpy as jnp
        import numpy as np
        N_NODES = 50000
        N_EDGES = 50000
        DIM = 128
        SLOPE = 0.2
        src, dst = (indices[0], indices[1])
        d = W1_w.shape[1]
        h_att = features @ Watt_w + Watt_b
        a1, a2 = (a[:d], a[d:])
        e = jax.nn.leaky_relu(h_att[src] @ a1 + h_att[dst] @ a2, SLOPE)
        e = e - jnp.max(e)
        exp_e = jnp.exp(e)
        denom = jax.ops.segment_sum(exp_e, dst, num_segments=num_nodes)
        alpha = exp_e / (denom[dst] + 1e-09)
        h_msg = features @ W1_w + W1_b
        weighted = h_msg[src] * alpha
        h_neigh = jax.ops.segment_sum(weighted, dst, num_segments=num_nodes)
        h_self = features
        sum_h = h_self + h_neigh
        prod_h = h_self * h_neigh
        return jax.nn.leaky_relu(sum_h + prod_h @ W2_w + W2_b, SLOPE)
    edge_index = jnp.stack([src, dst])
    x = _layernorm(x + _L0_gnn_ref(x, edge_attr_20, edge_weight, src, dst, L0_gnn_W_in, L0_gnn_b_in, L0_gnn_Wf1, L0_gnn_bf1, L0_gnn_Wf2, L0_gnn_bf2, L0_gnn_Wo1, L0_gnn_bo1, L0_gnn_Wo2, L0_gnn_bo2), axis=-1)
    x = _layernorm(x + _L1_gnn_ref(edge_index, x, 3125, L1_gnn_W1_w, L1_gnn_W1_b, L1_gnn_W2_w, L1_gnn_W2_b, L1_gnn_Watt_w, L1_gnn_Watt_b, L1_gnn_a), axis=-1)
    return x

_drawn_inputs = setup_inputs


def setup_inputs(seed=0):
    import zlib

    import numpy as np

    out = dict(_drawn_inputs(seed))
    spreads = {'L0_gnn_b_in': (0.0, 0.275),
     'L0_gnn_bf1': (0.0, 0.768),
     'L0_gnn_bf2': (0.0, 0.41),
     'L0_gnn_bo1': (0.0, 2.0),
     'L0_gnn_bo2': (0.0, 0.8)}
    factors = {'edge_attr_20': 8.0,
     'edge_weight': 3.139,
     'L0_gnn_Wf1': 4.096,
     'L0_gnn_Wf2': 3.863,
     'L1_gnn_Watt_w': 4.788,
     'L1_gnn_Watt_b': 200.0,
     'L1_gnn_a': 4.962}
    for name, (base, spread) in spreads.items():
        noise = np.random.default_rng([zlib.crc32(name.encode()), seed]).standard_normal(out[name].shape)
        drawn = base * np.exp(spread * noise) if base else spread * noise
        out[name] = jnp.asarray(drawn.astype(out[name].dtype))
    for name, factor in factors.items():
        out[name] = (out[name] * factor).astype(out[name].dtype)
    return out
```

```python
from contextlib import ExitStack

import concourse.bass as bass
from concourse import mybir

F32 = mybir.dt.float32
BF16 = mybir.dt.bfloat16
I32 = mybir.dt.int32
I16 = mybir.dt.int16
ALU = mybir.AluOpType
ACT = mybir.ActivationFunctionType
AX = mybir.AxisListType.X

P = 128
N, D = 3125, 128
NB = -(-N // P)
NP = NB * P
CB = 5
NC = NB // CB
CN = CB * P
E, RBF = 103125, 20
WG = 1024
NG = -(-E // WG)
EP = NG * WG
NT = EP // P
HALF = 512
TQ = HALF // P
TG = WG // P
PAD_DST = 4095
TROWS = -(-(N + P) // P) * P
HROW = 132
RING = 4
IDX_COLS = -(-NG // RING) * RING * TG
LN2 = 0.6931471805599453
EPS = 1e-5
SLOPE = 0.2
LOW = -1e30
FAR = 80.0


def build(nc, a, out):
    ctx = ExitStack()
    with ctx:
        def sb(name, shape, dt=F32):
            return ctx.enter_context(nc.sbuf_tensor(name, shape, dt))

        def sem(name):
            return ctx.enter_context(nc.semaphore(name))

        def sems(name, n):
            return [sem(f"{name}{k}") for k in range(n)]

        def dram(name, shape, dt=F32):
            return nc.dram_tensor(name, shape, dt).ap()

        sum_table = [dram(f"sum_table{q}", [TROWS, D]) for q in range(TQ)]
        h_table = dram("h_table", [NP, 3 * D], BF16)
        msg_table = dram("msg_table", [NP, HROW])
        src16 = dram("src16", [EP], I16)
        dst16 = dram("dst16", [EP], I16)
        cf_parts = dram("cf_parts", [3, 2 * D], BF16)

        passed = sem("passed")

        def stand_alone(eng):
            eng.sem_inc(passed, 1)

        ps_v = ctx.enter_context(nc.psum_tensor("ps_v", [P, 2, 512], F32))
        ps_wh = ctx.enter_context(nc.psum_tensor("ps_wh", [P, 2, 2, 512], F32))
        ps_d = ctx.enter_context(nc.psum_tensor("ps_d", [P, 2, 512], F32))
        ps_v_flat = ps_v[:, :, :].rearrange("p a n -> p (a n)")
        ps_d_flat = ps_d[:, :, :].rearrange("p a n -> p (a n)")

        ident = sb("ident", [P, P])
        ltri = sb("ltri", [P, P])
        iota_i = sb("iota_i", [P, P], I32)
        iota_f = sb("iota_f", [P, P])
        pcol_i = sb("pcol_i", [P, 1], I32)
        pcol = sb("pcol", [P, 1])
        win_i = sb("win_i", [P, NB], I32)
        win_off = sb("win_off", [P, NB])
        trash = sb("trash", [P, 1])
        ones = sb("ones", [P, P])
        ones_row = sb("ones_row", [1, 512])
        ones3 = sb("ones3", [3, P], BF16)
        neg_ln2 = sb("neg_ln2", [P, 1])
        w_in = sb("w_in", [P, D])
        wf1 = sb("wf1", [RBF + 1, D])
        wf2 = sb("wf2", [P, D])
        wo1 = sb("wo1", [P, D])
        wo2 = sb("wo2", [P, D])
        w1x = sb("w1x", [P, HROW])
        w2 = sb("w2", [P, D])
        watt_t = sb("watt_t", [P, D])
        att2 = sb("att2", [P, 2])
        att_sum = sb("att_sum", [P, 1])
        batt = sb("batt", [P, 1])
        bo1 = sb("bo1", [P, 1])
        b_in = sb("b_in", [1, D])
        bf2 = sb("bf2", [1, D])
        bo2 = sb("bo2", [1, D])
        b1x = sb("b1x", [1, HROW])
        b2 = sb("b2", [1, D])
        c2row = sb("c2row", [1, D])
        cf_row = sb("cf_row", [1, D])
        cf_left = sb("cf_left", [1, D])
        cf_split = sb("cf_split", [1, 3, 2, D], BF16)
        cf3 = sb("cf3", [3, 2 * D], BF16)
        wa2b = sb("wa2b", [P, P])
        src_col = sb("src_col", [P, IDX_COLS], I32)
        dst_col = sb("dst_col", [P, NT], I32)
        src_f = sb("src_f", [P, NT])
        src_less_trash = sb("src_less_trash", [P, NT])
        dst_f = sb("dst_f", [P, NT])
        pad_low = sb("pad_low", [P, NT])
        w_col = sb("w_col", [P, NT])
        dst_lo = sb("dst_lo", [NG, 1])
        dst_hi = sb("dst_hi", [NG, 1])
        lo_row = sb("lo_row", [1, NG])
        span = sb("span", [1, NG])
        span_max = sb("span_max", [1, 1])
        reached = sb("reached", [1, NB])
        extra = sb("extra", [1, 1])
        top = sb("top", [1, 1])
        base_row = sb("base_row", [1, NG])
        ctrl = sb("ctrl", [1, NG + 1], I32)
        base_b = sb("base_b", [P, NG])
        base_p = sb("base_p", [P, NG])
        x1 = sb("x1", [P, NB, D])
        x1_t = sb("x1_t", [P, NP])
        ln_var = sb("ln_var", [P, NB])
        ln_mean = sb("ln_mean", [P, NB])
        ln_std = sb("ln_std", [P, NB])
        ln_rstd = sb("ln_rstd", [P, NB])

        def window(first, w):
            start = nc.s_assert_within(first + w * P, 0, NP - P, skip_runtime_bounds_check_because=(
                "base_row is at most NP - P * (number of windows)"))
            return bass.ds(start, P)

        def need(eng, s, count):
            if not isinstance(count, int) or count > 0:
                eng.wait_ge(s, count)

        def value(eng, ap, hi, lo=0):
            return eng.value_load(ap, min_val=lo, max_val=hi)

        with ExitStack() as prep:
            def tmp(name, shape, dt=F32):
                return prep.enter_context(nc.sbuf_tensor(name, shape, dt))

            x_t = tmp("x_t", [P, NP])
            h3 = tmp("h3", [P, NB, 3 * D], BF16)
            h_left = tmp("h_left", [P, CB, D])
            zero = tmp("zero", [P, TROWS // P * D])
            flat_src = tmp("flat_src", [P, NT], I32)
            flat_dst = tmp("flat_dst", [P, NT], I32)
            flat_src16 = tmp("flat_src16", [P, NT], I16)
            flat_dst16 = tmp("flat_dst16", [P, NT], I16)
            lo_in = tmp("lo_in", [NG, WG], I32)
            hi_in = tmp("hi_in", [NG, WG], I32)

            consts_in = sem("consts_in")
            edges_in = sem("edges_in")
            flats_in = sem("flats_in")
            x_in = sem("x_in")
            range_in = sem("range_in")
            range_fill = sem("range_fill")
            wrote = sem("wrote")
            cf_back = sem("cf_back")
            pool_made = sem("pool_made")
            zero_made = sem("zero_made")
            w1x_zero = sem("w1x_zero")
            flat_cast = sem("flat_cast")
            cols_made = sem("cols_made")
            h_mm = sem("h_mm")
            h_hi = sem("h_hi")
            h_rest = sem("h_rest")
            h_mid = sem("h_mid")
            h_lo = sem("h_lo")
            small = sem("small")
            small_mm = sem("small_mm")
            cf_ready = sem("cf_ready")

            n_consts = 0
            block = prep.enter_context(nc.Block())
            row = lambda ap: ap.rearrange("(a n) -> a n", a=1)
            col = lambda ap: ap.rearrange("(n a) -> n a", a=1)
            dst_rows = a["dst_row"].rearrange("(g n) -> g n", g=NG)
            tail = E - (NG - 1) * WG

            @block.sync
            def _(sp):
                sp.dma_start(x_t[:], a["x_t"]).then_inc(x_in, 16)
                sp.dma_start(w_in[:], a["L0_gnn_W_in"]).then_inc(x_in, 16)
                sp.dma_start(b_in[:], row(a["L0_gnn_b_in"])).then_inc(x_in, 16)
                sp.dma_start(flat_src[:], a["src_row"].rearrange("(p t) -> p t", p=P)).then_inc(flats_in, 16)
                sp.dma_start(flat_dst[:], a["dst_row"].rearrange("(p t) -> p t", p=P)).then_inc(flats_in, 16)
                sp.wait_ge(range_fill, 2)
                for t in (lo_in, hi_in):
                    sp.dma_start(t[0:NG - 1, :], dst_rows[0:NG - 1, :]).then_inc(range_in, 16)
                    sp.dma_start(t[NG - 1:NG, 0:tail], dst_rows[NG - 1:NG, 0:tail]).then_inc(range_in, 16)
                sp.wait_ge(flat_cast, 2)
                sp.dma_start(src16.rearrange("(p t) -> p t", p=P), flat_src16[:]).then_inc(wrote, 16)
                sp.dma_start(dst16.rearrange("(p t) -> p t", p=P), flat_dst16[:]).then_inc(wrote, 16)
                sp.wait_ge(zero_made, 1)
                for q in range(TQ):
                    sp.dma_start(sum_table[q].rearrange("(p r) d -> p (r d)", p=P), zero[:]).then_inc(wrote, 16)
                sp.wait_ge(cf_ready, 3)
                sp.dma_start(cf_parts, cf_split[:, :, :, :].rearrange("a k c d -> a k (c d)")).then_inc(cf_back, 16)
                sp.wait_ge(cf_back, 16)
                sp.dma_start(cf3[:], cf_parts).then_inc(cf_back, 16)
                sp.wait_ge(h_lo, NC)
                sp.dma_start(h_table.rearrange("(b p) f -> p b f", p=P), h3[:, :, :]).then_inc(wrote, 16)
                sp.wait_ge(cf_back, 32)
                sp.wait_ge(wrote, 16 * (TQ + 3))

            CONST_LOADS = [
                (wf1[0:RBF, :], a["L0_gnn_Wf1"]), (wf1[RBF:RBF + 1, :], row(a["L0_gnn_bf1"])),
                (wf2[:], a["L0_gnn_Wf2"]), (bf2[:], row(a["L0_gnn_bf2"])),
                (wo1[:], a["L0_gnn_Wo1"]), (bo1[:], col(a["L0_gnn_bo1"])),
                (wo2[:], a["L0_gnn_Wo2"]), (bo2[:], row(a["L0_gnn_bo2"])),
                (watt_t[:], a["watt_t"]), (batt[:], col(a["L1_gnn_Watt_b"])), (att2[:], a["att2"]),
                (w2[:], a["L1_gnn_W2_w"]), (b2[:], row(a["L1_gnn_W2_b"])),
            ]
            n_consts = len(CONST_LOADS) + 2

            @block.scalar
            def _(act):
                for dst, src in CONST_LOADS:
                    act.dma_start(dst, src).then_inc(consts_in, 16)
                for dst, src in ((src_col, "src_col"), (dst_col, "dst_col"), (w_col, "w_col")):
                    act.dma_start(dst[:, 0:NT], a[src]).then_inc(edges_in, 16)
                act.wait_ge(w1x_zero, 2)
                act.dma_start(w1x[:, 0:D], a["L1_gnn_W1_w"]).then_inc(consts_in, 16)
                act.dma_start(b1x[:, 0:D], row(a["L1_gnn_W1_b"])).then_inc(consts_in, 16)
                for c in range(NC):
                    act.wait_ge(h_mm, c + 1)
                    nc.scalar.activation(h3[:, c * CB:(c + 1) * CB, 0:D],
                                         ps_v_flat[:, 0:CN].rearrange("p (b d) -> p b d", d=D),
                                         ACT.Copy).then_inc(h_hi, 1)
                    act.wait_ge(h_rest, c + 1)
                    nc.scalar.activation(h3[:, c * CB:(c + 1) * CB, D:2 * D], h_left[:, :, :],
                                         ACT.Copy).then_inc(h_mid, 1)

            @block.gpsimd
            def _(pool):
                nc.gpsimd.memset(ident[:], 0.0).then_inc(pool_made, 1)
                nc.gpsimd.memset(ltri[:], 1.0).then_inc(pool_made, 1)
                pool.wait_ge(pool_made, 2)
                nc.gpsimd.affine_select(out=ident[:], in_=ident[:], compare_op=ALU.not_equal, fill=1.0, base=0,
                                        pattern=[[-1, P]], channel_multiplier=1).then_inc(pool_made, 1)
                nc.gpsimd.affine_select(out=ltri[:], in_=ltri[:], compare_op=ALU.is_ge, fill=0.0, base=0,
                                        pattern=[[-1, P]], channel_multiplier=1).then_inc(pool_made, 1)
                nc.gpsimd.iota(iota_i[:], [[1, P]], base=0, channel_multiplier=0).then_inc(pool_made, 1)
                nc.gpsimd.iota(pcol_i[:], [[1, 1]], base=0, channel_multiplier=1).then_inc(pool_made, 1)
                nc.gpsimd.iota(win_i[:], [[P, NB]], base=0, channel_multiplier=0).then_inc(pool_made, 1)
                nc.gpsimd.memset(zero[:], 0.0).then_inc(zero_made, 1)
                if IDX_COLS > NT:
                    nc.gpsimd.memset(src_col[:, NT:IDX_COLS], 0)

            @block.tensor
            def _(pe):
                pe.wait_ge(x_in, 48)
                pe.wait_ge(small, 1)
                for c in range(NC):
                    if c:
                        need(pe, h_rest, c)
                    for b in range(CB):
                        o = ps_v_flat[:, b * P:(b + 1) * P]
                        k = (c * CB + b) * P
                        nc.tensor.matmul(o, x_t[:, k:k + P], w_in[:], start=True, stop=False)
                        mm = nc.tensor.matmul(o, ones_row[:, 0:P], b_in[:], start=False, stop=True)
                    mm.then_inc(h_mm, 1)
                pe.wait_ge(consts_in, 16 * n_consts)
                pe.wait_ge(small, 3)
                pe.wait_ge(pool_made, 7)
                s = ps_wh[:, 0, 0, :]
                nc.tensor.matmul(s[0:1, 0:D], neg_ln2[:], wf2[:], start=True, stop=False)
                nc.tensor.matmul(s[0:1, 0:D], ones_row[:, 0:1], bf2[:], start=False, stop=True)
                nc.tensor.matmul(s[0:1, D:2 * D], neg_ln2[:], wo2[:], start=True, stop=False)
                nc.tensor.matmul(s[0:1, D:2 * D], ones_row[:, 0:1], bo2[:], start=False, stop=True)
                nc.tensor.matmul(s[:, 256:258], watt_t[:], att2[:], start=True, stop=True)
                nc.tensor.matmul(s[0:1, 260:261], batt[:], att_sum[:], start=True, stop=True).then_inc(small_mm, 1)
                pe.wait_ge(small, 5)
                r = ps_wh[:, 0, 1, :]
                nc.tensor.matmul(r[0:1, 0:NG], dst_lo[:], ident[0:NG, 0:NG], start=True, stop=True)
                nc.tensor.matmul(r[0:1, P:P + NG], dst_hi[:], ident[0:NG, 0:NG], start=True,
                                 stop=True).then_inc(small_mm, 1)
                pe.wait_ge(small, 15)
                nc.tensor.matmul(r[:, 256:256 + NG], ones_row[:, 0:P], base_row[:], start=True,
                                 stop=True).then_inc(small_mm, 1)

            @block.vector
            def _(dve):
                done = [0]

                def link(ins):
                    done[0] += 1
                    ins.then_inc(small, 1)
                    dve.wait_ge(small, done[0])

                link(nc.vector.memset(ones_row[:], 1.0))
                nc.vector.memset(lo_in[:], N - 1).then_inc(range_fill, 1)
                nc.vector.memset(hi_in[:], 0).then_inc(range_fill, 1)
                nc.vector.memset(w1x[:], 0.0).then_inc(w1x_zero, 1)
                nc.vector.memset(b1x[:], 0.0).then_inc(w1x_zero, 1)
                nc.vector.memset(ones[:], 1.0)
                nc.vector.memset(ones3[:], 1.0)
                link(nc.vector.memset(neg_ln2[:], -LN2))
                dve.wait_ge(flats_in, 32)
                nc.vector.tensor_copy(flat_src16[:], flat_src[:]).then_inc(flat_cast, 1)
                nc.vector.tensor_copy(flat_dst16[:], flat_dst[:]).then_inc(flat_cast, 1)
                dve.wait_ge(consts_in, 16 * n_consts)
                link(nc.vector.tensor_tensor(att_sum[:], att2[:, 0:1], att2[:, 1:2], ALU.add))
                for c in range(NC):
                    dve.wait_ge(h_hi, c + 1)
                    if c:
                        need(dve, h_mid, c)
                        need(dve, h_lo, c)
                    nc.vector.tensor_tensor(h_left[:, :, :], ps_v_flat[:, 0:CN].rearrange("p (b d) -> p b d", d=D),
                                            h3[:, c * CB:(c + 1) * CB, 0:D], ALU.subtract).then_inc(h_rest, 1)
                    dve.wait_ge(h_mid, c + 1)
                    dve.wait_ge(h_rest, c + 1)
                    nc.vector.tensor_tensor(h3[:, c * CB:(c + 1) * CB, 2 * D:3 * D], h_left[:, :, :],
                                            h3[:, c * CB:(c + 1) * CB, D:2 * D], ALU.subtract).then_inc(h_lo, 1)
                dve.wait_ge(range_in, 64)
                link(nc.vector.tensor_reduce(dst_lo[:], lo_in[:], AX, ALU.min))
                link(nc.vector.tensor_reduce(dst_hi[:], hi_in[:], AX, ALU.max))
                dve.wait_ge(pool_made, 7)
                nc.vector.tensor_copy(iota_f[:], iota_i[:])
                nc.vector.tensor_copy(win_off[:], win_i[:])
                link(nc.vector.tensor_copy(pcol[:], pcol_i[:]))
                link(nc.vector.tensor_scalar(trash[:], pcol[:], float(N), None, ALU.add))
                dve.wait_ge(small_mm, 2)
                r = ps_wh[:, 0, 1, :]
                link(nc.vector.tensor_copy(lo_row[:], r[0:1, 0:NG]))
                link(nc.vector.tensor_tensor(span[:], r[0:1, P:P + NG], lo_row[:], ALU.subtract))
                link(nc.vector.tensor_reduce(span_max[:], span[:], AX, ALU.max))
                link(nc.vector.tensor_scalar(reached[:, 1:NB], win_off[0:1, 1:NB], span_max[:, 0:1], None, ALU.is_le))
                link(nc.vector.tensor_reduce(extra[:], reached[:, 1:NB], AX, ALU.add))
                link(nc.vector.tensor_scalar(top[:], extra[:], -float(P), float(NP - P), ALU.mult, ALU.add))
                nc.vector.tensor_scalar(ctrl[:, NG:NG + 1], extra[:], 1.0, None, ALU.add)
                link(nc.vector.tensor_scalar(base_row[:], lo_row[:], top[:, 0:1], None, ALU.min))
                assert done[0] == 14
                link(nc.vector.tensor_copy(ctrl[:, 0:NG], base_row[:]))
                dve.wait_ge(small_mm, 3)
                link(nc.vector.tensor_copy(base_b[:], r[:, 256:256 + NG]))
                nc.vector.tensor_scalar(base_p[:], base_b[:], pcol[:, 0:1], None, ALU.add)
                dve.wait_ge(edges_in, 48)
                link(nc.vector.tensor_copy(src_f[:], src_col[:, 0:NT]))
                nc.vector.tensor_scalar(src_less_trash[:], src_f[:], trash[:, 0:1], None, ALU.subtract)
                link(nc.vector.tensor_copy(dst_f[:], dst_col[:]))
                nc.vector.tensor_scalar(pad_low[:], dst_f[:], float(PAD_DST - 1), LOW, ALU.is_gt, ALU.mult)
                s = ps_wh[:, 0, 0, :]
                nc.vector.tensor_copy(w1x[:, D:D + 1], s[:, 256:257])
                nc.vector.tensor_copy(b1x[:, D:D + 1], s[0:1, 260:261])
                nc.vector.tensor_scalar(wa2b[:], ones[:], s[:, 257:258], None, ALU.mult)
                nc.vector.tensor_copy(c2row[:], s[0:1, D:2 * D])
                link(nc.vector.tensor_copy(cf_row[:], s[0:1, 0:D]))
                left = cf_row
                for k in range(3):
                    for dup in range(2):
                        last = nc.vector.tensor_copy(cf_split[:, k, dup, :], left[:])
                    last.then_inc(cf_ready, 1)
                    if k < 2:
                        dve.wait_ge(cf_ready, k + 1)
                        link(nc.vector.tensor_tensor(cf_left[:], left[:], cf_split[:, k, 0, :], ALU.subtract))
                        left = cf_left

        with ExitStack() as conv:
            def tmp(name, shape, dt=F32):
                return conv.enter_context(nc.sbuf_tensor(name, shape, dt))

            f_t = tmp("f_t", [RBF + 1, 2, HALF])
            dst_bc = tmp("dst_bc", [P, 2, HALF], I16)
            src_bc = tmp("src_bc", [P, 2, HALF], I16)
            h_win = tmp("h_win", [P, 2, 3 * D], BF16)
            onehot_t = tmp("onehot_t", [P, 2, HALF], BF16)
            sp_abs = tmp("sp_abs", [P, HALF])
            sp_exp = tmp("sp_exp", [P, HALF])
            sp_log = tmp("sp_log", [P, 2, HALF])
            filt = tmp("filt", [P, 2, HALF])
            h_edge = tmp("h_edge", [P, 2, TQ, D])
            x_edge = tmp("x_edge", [P, 2, TQ, D])
            same = tmp("same", [P, 2, TQ, P])
            count = tmp("count", [P, 2, TQ])
            row_f = tmp("row_f", [P, 2, TQ])
            row_i = tmp("row_i", [P, 2, TQ], I32)
            rows_out = tmp("rows_out", [P, 2, TQ, D])

            f_in = sems("f_in", 2)
            dst_in = sems("dst_in", 2)
            src_in = sems("src_in", 2)
            win_in = sems("win_in", 2)
            f_ones = sem("f_ones")
            v_done = sems("v_done", 2)
            abs_done = sem("abs_done")
            exp_done = sem("exp_done")
            log_done = sems("log_done", 2)
            filt_done = sems("filt_done", 2)
            onehot_done = sems("onehot_done", 2)
            win_used = sems("win_used", 2)
            wh_done = sems("wh_done", 2)
            h_copied = sems("h_copied", 2)
            same_done = sems("same_done", 2)
            row_part = sems("row_part", 2)
            row_done = sems("row_done", 2)
            x_done = sems("x_done", 2)
            d_done = sems("d_done", 2)
            out_done = sems("out_done", 2)
            added = [sems(f"added{j}_", TQ) for j in range(2)]

            block = conv.enter_context(nc.Block())

            @block.sync
            def _(sp):
                n_win = value(sp, ctrl[0:1, NG:NG + 1], NB, 1)

                def load_f(i, j):
                    sp.dma_start(f_t[0:RBF, j, :], a["f_t"][:, bass.ds((i * 2 + j) * HALF, HALF)]).then_inc(f_in[j], 16)

                def step(i, j, last):
                    at = bass.ds((i * 2 + j) * HALF, HALF)
                    need(sp, onehot_done[j], i * n_win if not isinstance(i, int) or i else 0)
                    sp.dma_start(dst_bc[:, j, :], dst16[at].partition_broadcast(P)).then_inc(dst_in[j], 16)
                    first = value(sp, ctrl[0:1, bass.ds(i, 1)], NP - P)
                    with sp.Fori(0, n_win) as w:
                        sp.wait_ge(win_used[j], i * n_win + w + 1)
                        sp.dma_start(h_win[:, j, :], h_table[window(first, w), :]).then_inc(win_in[j], 16)
                    need(sp, same_done[j], i)
                    sp.dma_start(src_bc[:, j, :], src16[at].partition_broadcast(P)).then_inc(src_in[j], 16)
                    if not last:
                        sp.wait_ge(v_done[j], i + 1)
                        load_f(i + 1, j)

                sp.wait_ge(f_ones, 1)
                load_f(0, 0)
                load_f(0, 1)
                step(0, 0, False)
                step(0, 1, False)
                with sp.Fori(1, NG - 1) as i:
                    step(i, 0, False)
                    step(i, 1, False)
                step(NG - 1, 0, True)
                step(NG - 1, 1, True)

            @block.tensor
            def _(pe):
                n_win = value(pe, ctrl[0:1, NG:NG + 1], NB, 1)

                def hidden(i, j):
                    pe.wait_ge(f_in[j], (i + 1) * 16)
                    need(pe, filt_done[j], i)
                    nc.tensor.matmul(ps_v[:, j, :], wf1[:], f_t[:, j, :], start=True, stop=True).then_inc(v_done[j], 1)

                def filter_and_h(i, j):
                    need(pe, x_done[j], i)
                    need(pe, h_copied[j], i)
                    for k in range(2):
                        nc.tensor.matmul(ps_wh[:, j, k, 0:2 * D], ones3[:], cf3[:], start=True, stop=False,
                                         skip_group_check=True)
                    with pe.Fori(0, n_win) as w:
                        pe.wait_ge(win_in[j], (i * n_win + w + 1) * 16)
                        pe.wait_ge(onehot_done[j], i * n_win + w + 1)
                        for q in range(TQ):
                            o = ps_wh[:, j, q // 2, (2 + q % 2) * D:(3 + q % 2) * D]
                            for part in range(3):
                                mm = nc.tensor.matmul(o, onehot_t[:, j, q * P:(q + 1) * P],
                                                      h_win[:, j, part * D:(part + 1) * D], start=False, stop=False,
                                                      skip_group_check=True)
                        mm.then_inc(win_used[j], 1)
                    pe.wait_ge(filt_done[j], i + 1)
                    for q in range(TQ):
                        mm = nc.tensor.matmul(ps_wh[:, j, q // 2, q % 2 * D:(q % 2 + 1) * D],
                                              filt[:, j, q * P:(q + 1) * P], wf2[:], start=False, stop=True,
                                              skip_group_check=True)
                    mm.then_inc(wh_done[j], 1)

                def merge(i, j):
                    pe.wait_ge(same_done[j], i + 1)
                    pe.wait_ge(x_done[j], i + 1)
                    need(pe, out_done[j], i)
                    for q in range(TQ):
                        mm = nc.tensor.matmul(ps_d[:, j, q * D:(q + 1) * D], same[:, j, q, :], x_edge[:, j, q, :],
                                              start=True, stop=True)
                    mm.then_inc(d_done[j], 1)

                def steps(i, first, last):
                    for j in range(2):
                        filter_and_h(i, j)
                        if not last:
                            hidden(i + 1, j)
                        if j:
                            merge(i, 0)
                        elif not first:
                            merge(i - 1, 1)

                for j in range(2):
                    pe.sem_inc(win_used[j], 1)
                hidden(0, 0)
                hidden(0, 1)
                steps(0, True, False)
                steps(1, False, False)
                with pe.Fori(2, NG - 1) as i:
                    steps(i, False, False)
                steps(NG - 1, False, True)
                merge(NG - 1, 1)

            @block.scalar
            def _(act):
                def softplus(i, j):
                    n = i * 2 + j + 1
                    act.wait_ge(v_done[j], i + 1)
                    nc.scalar.activation(sp_abs[:], ps_v[:, j, :], ACT.Abs).then_inc(abs_done, 1)
                    act.wait_ge(abs_done, n)
                    nc.scalar.activation(sp_exp[:], sp_abs[:], ACT.Exp, scale=-1.0).then_inc(exp_done, 1)
                    act.wait_ge(exp_done, n)
                    need(act, filt_done[j], i)
                    nc.scalar.activation(sp_log[:, j, :], sp_exp[:], ACT.Ln, bias=1.0).then_inc(log_done[j], 1)

                def copy_h(i, j):
                    act.wait_ge(wh_done[j], i + 1)
                    need(act, x_done[j], i)
                    nc.scalar.activation(h_edge[:, j, :, :].rearrange("p (k q) d -> p k (q d)", k=2),
                                         ps_wh[:, j, :, 2 * D:4 * D], ACT.Copy).then_inc(h_copied[j], 1)

                def copy_rows(i, j):
                    act.wait_ge(d_done[j], i + 1)
                    for q in range(TQ):
                        need(act, added[j][q], i * 16)
                    nc.scalar.activation(rows_out[:, j, :, :].rearrange("p q d -> p (q d)"), ps_d[:, j, :],
                                         ACT.Copy).then_inc(out_done[j], 1)

                def steps(i, first, last):
                    for j in range(2):
                        copy_h(i, j)
                        if not last:
                            softplus(i + 1, j)
                        if j:
                            copy_rows(i, 0)
                        elif not first:
                            copy_rows(i - 1, 1)

                softplus(0, 0)
                softplus(0, 1)
                steps(0, True, False)
                steps(1, False, False)
                with act.Fori(2, NG - 1) as i:
                    steps(i, False, False)
                steps(NG - 1, False, True)
                copy_rows(NG - 1, 1)

            @block.vector
            def _(dve):
                n_win = value(dve, ctrl[0:1, NG:NG + 1], NB, 1)

                def onehots(i, j):
                    dve.wait_ge(dst_in[j], (i + 1) * 16)
                    stand_alone(dve)
                    with dve.Fori(0, n_win) as w:
                        dve.wait_ge(win_used[j], i * n_win + w + 1)
                        nc.vector.tensor_scalar(onehot_t[:, j, :], dst_bc[:, j, :], base_p[:, bass.ds(i, 1)],
                                                win_off[:, bass.ds(w, 1)], ALU.subtract,
                                                ALU.is_equal).then_inc(onehot_done[j], 1)

                def filters(i, j):
                    dve.wait_ge(log_done[j], i + 1)
                    need(dve, wh_done[j], i)
                    nc.vector.scalar_tensor_tensor(filt[:, j, :], ps_v[:, j, :], 0.0, sp_log[:, j, :], ALU.max,
                                                   ALU.add).then_inc(filt_done[j], 1)

                def rows(i, j):
                    dve.wait_ge(src_in[j], (i + 1) * 16)
                    need(dve, d_done[j], i)
                    for q in range(TQ):
                        t = i * TG + j * TQ + q
                        ins = nc.vector.scalar_tensor_tensor(same[:, j, q, :], src_bc[:, j, q * P:(q + 1) * P],
                                                             src_f[:, bass.ds(t, 1)], ltri[:], ALU.is_equal,
                                                             ALU.mult, accum_out=count[:, j, q:q + 1])
                    ins.then_inc(same_done[j], 1)
                    dve.wait_ge(same_done[j], i + 1)
                    nc.vector.scalar_tensor_tensor(row_f[:, j, :], count[:, j, :], 1.0,
                                                   src_less_trash[:, bass.ds(i * TG + j * TQ, TQ)], ALU.is_equal,
                                                   ALU.mult).then_inc(row_part[j], 1)
                    dve.wait_ge(row_part[j], i + 1)
                    for q in range(TQ):
                        need(dve, added[j][q], i * 16)
                    nc.vector.tensor_scalar(row_i[:, j, :], row_f[:, j, :], trash[:, 0:1], None,
                                            ALU.add).then_inc(row_done[j], 1)

                def products(i, j):
                    dve.wait_ge(h_copied[j], i + 1)
                    for q in range(TQ):
                        t = i * TG + j * TQ + q
                        ins = nc.vector.scalar_tensor_tensor(x_edge[:, j, q, :],
                                                             ps_wh[:, j, q // 2, q % 2 * D:(q % 2 + 1) * D],
                                                             w_col[:, bass.ds(t, 1)], h_edge[:, j, q, :], ALU.mult,
                                                             ALU.mult)
                    ins.then_inc(x_done[j], 1)

                def steps(i, last):
                    for j in range(2):
                        if j == 0:
                            onehots(i, 1)
                            filters(i, 1)
                        elif not last:
                            onehots(i + 1, 0)
                            filters(i + 1, 0)
                        rows(i, j)
                        products(i, j)

                nc.vector.memset(f_t[:, :, :], 1.0).then_inc(f_ones, 1)
                onehots(0, 0)
                filters(0, 0)
                steps(0, False)
                with dve.Fori(1, NG - 1) as i:
                    steps(i, False)
                steps(NG - 1, True)

            @block.gpsimd
            def _(pool):
                def step(i, j):
                    pool.wait_ge(out_done[j], i + 1)
                    pool.wait_ge(row_done[j], i + 1)
                    for q in range(TQ):
                        if j:
                            pool.wait_ge(added[0][q], (i + 1) * 16)
                        else:
                            need(pool, added[1][q], i * 16)
                        stand_alone(pool)
                        pool.indirect_dma_start(sum_table[q], bass.IndirectOffsetOnAxis(row_i[:, j, q:q + 1], 0),
                                                rows_out[:, j, q, :], None,
                                                compute_op=ALU.add).then_inc(added[j][q], 16)

                step(0, 0)
                step(0, 1)
                with pool.Fori(1, NG) as i:
                    step(i, 0)
                    step(i, 1)
                for j in range(2):
                    for q in range(TQ):
                        pool.wait_ge(added[j][q], NG * 16)

        s2_b = sb("s2_b", [P, NP])
        acc = sb("acc", [P, 2, NP])
        ref = sb("ref", [P, NP])

        def stats(dve, src, st, mv, c, stat_done, aggr_done):
            for b in range(CB):
                ins = nc.vector.bn_stats(st[:, b, :], src[:, bass.ds(c * CB + b, 1), :].rearrange("p a d -> p (a d)"))
            ins.then_inc(stat_done, 1)
            dve.wait_ge(stat_done, c + 1)
            for b in range(CB):
                ins = nc.vector.bn_aggr(mv[:, b, :], st[:, b, :])
            ins.then_inc(aggr_done, 1)
            dve.wait_ge(aggr_done, c + 1)
            nc.vector.tensor_copy(ln_mean[:, bass.ds(c * CB, CB)], mv[:, :, 0])
            return nc.vector.tensor_scalar(ln_var[:, bass.ds(c * CB, CB)], mv[:, :, 1], EPS, None, ALU.add)

        with ExitStack() as nodes:
            def tmp(name, shape, dt=F32):
                return nodes.enter_context(nc.sbuf_tensor(name, shape, dt))

            tables = tmp("tables", [P, TQ, CB, D])
            agg_t = tmp("agg_t", [P, CN])
            n_abs = tmp("n_abs", [P, 2, CN // 2])
            n_exp = tmp("n_exp", [P, 2, CN // 2])
            n_log = tmp("n_log", [P, 2, CN // 2])
            n_pos = tmp("n_pos", [P, 2, CN // 2])
            n_sp = tmp("n_sp", [P, CN])
            st = tmp("st", [P, CB, 6])
            mv = tmp("mv", [P, CB, 2])
            msg = tmp("msg", [P, NB, HROW])

            x_in = sem("x_node_in")
            tab_in = sem("tab_in")
            agg_mm = sem("agg_mm")
            agg_sb = sem("agg_sb")
            o1_mm = sem("o1_mm")
            o1_abs = sem("o1_abs")
            o1_exp = sem("o1_exp")
            o1_log = sem("o1_log")
            o1_pos = sem("o1_pos")
            o1_sp = sem("o1_sp")
            z_mm = sem("z_mm")
            z_sum = sem("z_sum")
            stat_done = sem("stat_done")
            aggr_done = sem("aggr_done")
            var_done = sem("var_done")
            std_done = sem("std_done")
            rstd_done = sem("rstd_done")
            x1_done = sem("x1_done")
            xt_mm = sem("xt_mm")
            xt_done = sem("xt_done")
            msg_mm = sem("msg_mm")
            msg_done = sem("msg_done")
            s2_done = sem("s2_done")
            msg_out = sem("msg_out")

            block = nodes.enter_context(nc.Block())

            @block.sync
            def _(sp):
                sp.dma_start(x1[:, :, :], a["x_rows"].rearrange("(b p) d -> p b d", p=P)).then_inc(x_in, 16)
                for c in range(NC):
                    need(sp, agg_mm, c)
                    for q in range(TQ):
                        sp.dma_start(tables[:, q, :, :],
                                     sum_table[q][bass.ds(c * CN, CN), :].rearrange("(b p) d -> p b d", p=P)
                                     ).then_inc(tab_in, 16)
                for c in range(NC):
                    sp.wait_ge(msg_done, c + 1)
                    sp.dma_start(msg_table[bass.ds(c * CN, CN), :].rearrange("(b p) d -> p b d", p=P),
                                 msg[:, bass.ds(c * CB, CB), :]).then_inc(msg_out, 16)
                sp.wait_ge(msg_out, NC * 16)

            @block.gpsimd
            def _(pool):
                nc.gpsimd.memset(acc[:, :, :], 0.0)
                nc.gpsimd.memset(ref[:], LOW)

            @block.tensor
            def _(pe):
                for c in range(NC):
                    pe.wait_ge(tab_in, (c + 1) * (16 * TQ))
                    need(pe, agg_sb, c)
                    for b in range(CB):
                        for q in range(TQ):
                            mm = nc.tensor.matmul(ps_v_flat[:, b * P:(b + 1) * P], tables[:, q, b, :], ident[:],
                                                  start=q == 0, stop=q == TQ - 1)
                    mm.then_inc(agg_mm, 1)
                    pe.wait_ge(agg_sb, c + 1)
                    need(pe, o1_sp, c)
                    for k in range(2):
                        mm = nc.tensor.matmul(ps_wh[:, 0, k, 0:CN // 2], wo1[:],
                                              agg_t[:, k * (CN // 2):(k + 1) * (CN // 2)], start=True, stop=True)
                    mm.then_inc(o1_mm, 1)
                    pe.wait_ge(o1_sp, c + 1)
                    need(pe, z_sum, c)
                    for b in range(CB):
                        o = ps_d_flat[:, b * P:(b + 1) * P]
                        nc.tensor.matmul(o, n_sp[:, b * P:(b + 1) * P], wo2[:], start=True, stop=False)
                        mm = nc.tensor.matmul(o, ones_row[:, 0:P], c2row[:], start=False, stop=True)
                    mm.then_inc(z_mm, 1)
                for c in range(NC):
                    pe.wait_ge(x1_done, c + 1)
                    need(pe, xt_done, c)
                    for b in range(CB):
                        mm = nc.tensor.matmul(ps_v_flat[:, b * P:(b + 1) * P],
                                              x1[:, c * CB + b, :], ident[:], start=True, stop=True)
                    mm.then_inc(xt_mm, 1)
                    pe.wait_ge(xt_done, c + 1)
                    need(pe, msg_done, c)
                    need(pe, s2_done, c)
                    for b in range(CB):
                        o = ps_wh[:, 0, b // 3, b % 3 * HROW:(b % 3 + 1) * HROW]
                        nc.tensor.matmul(o, x1_t[:, c * CN + b * P:c * CN + (b + 1) * P], w1x[:], start=True, stop=False)
                        nc.tensor.matmul(o, ones_row[:, 0:P], b1x[:], start=False, stop=True)
                    for k in range(2):
                        mm = nc.tensor.matmul(ps_d[:, k, 0:CN // 2], wa2b[:],
                                              x1_t[:, bass.ds(c * CN + k * (CN // 2), CN // 2)], start=True, stop=True)
                    mm.then_inc(msg_mm, 1)

            @block.scalar
            def _(act):
                for c in range(NC):
                    act.wait_ge(o1_mm, c + 1)
                    need(act, o1_sp, c)
                    nc.scalar.activation(n_abs[:, :, :], ps_wh[:, 0, :, 0:CN // 2], ACT.Abs,
                                         bias=bo1[:, 0:1]).then_inc(o1_abs, 1)
                    act.wait_ge(o1_abs, c + 1)
                    nc.scalar.activation(n_exp[:, :, :], n_abs[:, :, :], ACT.Exp, scale=-1.0).then_inc(o1_exp, 1)
                    act.wait_ge(o1_exp, c + 1)
                    nc.scalar.activation(n_log[:, :, :], n_exp[:, :, :], ACT.Ln, bias=1.0).then_inc(o1_log, 1)
                act.wait_ge(var_done, NC)
                nc.scalar.activation(ln_std[:], ln_var[:], ACT.Sqrt).then_inc(std_done, 1)
                for c in range(NC):
                    act.wait_ge(xt_mm, c + 1)
                    nc.scalar.activation(x1_t[:, bass.ds(c * CN, CN)], ps_v_flat[:, 0:CN], ACT.Copy).then_inc(xt_done, 1)
                    act.wait_ge(msg_mm, c + 1)
                    nc.scalar.activation(msg[:, bass.ds(c * CB, 3), :].rearrange("p b d -> p (b d)"),
                                         ps_wh[:, 0, 0, 0:3 * HROW], ACT.Copy)
                    nc.scalar.activation(msg[:, bass.ds(c * CB + 3, 2), :].rearrange("p b d -> p (b d)"),
                                         ps_wh[:, 0, 1, 0:2 * HROW], ACT.Copy).then_inc(msg_done, 1)

            @block.vector
            def _(dve):
                dve.wait_ge(x_in, 16)
                for c in range(NC):
                    dve.wait_ge(agg_mm, c + 1)
                    need(dve, o1_mm, c)
                    nc.vector.tensor_copy(agg_t[:], ps_v_flat[:, 0:CN]).then_inc(agg_sb, 1)
                    dve.wait_ge(o1_abs, c + 1)
                    nc.vector.tensor_scalar(n_pos[:, :, :], ps_wh[:, 0, :, 0:CN // 2], bo1[:, 0:1], 0.0, ALU.add,
                                            ALU.max).then_inc(o1_pos, 1)
                    dve.wait_ge(o1_pos, c + 1)
                    dve.wait_ge(o1_log, c + 1)
                    need(dve, z_mm, c)
                    nc.vector.tensor_tensor(n_sp[:].rearrange("p (k n) -> p k n", k=2), n_pos[:, :, :],
                                            n_log[:, :, :], ALU.add).then_inc(o1_sp, 1)
                    dve.wait_ge(z_mm, c + 1)
                    xs = x1[:, bass.ds(c * CB, CB), :]
                    nc.vector.tensor_tensor(xs, ps_d_flat[:, 0:CN].rearrange("p (b d) -> p b d", d=D), xs,
                                            ALU.add).then_inc(z_sum, 1)
                    dve.wait_ge(z_sum, c + 1)
                    stats(dve, x1, st, mv, c, stat_done, aggr_done).then_inc(var_done, 1)
                dve.wait_ge(std_done, 1)
                nc.vector.reciprocal(ln_rstd[:], ln_std[:]).then_inc(rstd_done, 1)
                dve.wait_ge(rstd_done, 1)
                for c in range(NC):
                    for b in range(CB):
                        k = bass.ds(c * CB + b, 1)
                        xs = x1[:, k, :].rearrange("p a d -> p (a d)")
                        ins = nc.vector.tensor_scalar(xs, xs, ln_mean[:, k], ln_rstd[:, k], ALU.subtract, ALU.mult)
                    ins.then_inc(x1_done, 1)
                    dve.wait_ge(msg_mm, c + 1)
                    nc.vector.tensor_copy(s2_b[:, bass.ds(c * CN, CN)].rearrange("p (k n) -> p k n", k=2),
                                          ps_d[:, :, 0:CN // 2]).then_inc(s2_done, 1)

        final_max = sb("final_max", [P, 1])
        with ExitStack() as att:
            def tmp(name, shape, dt=F32):
                return att.enter_context(nc.sbuf_tensor(name, shape, dt))

            rows_in = tmp("rows_in", [P, RING, TG, HROW])
            src_idx = tmp("src_idx", [P, RING, TG], I32)
            rel_a = tmp("rel_a", [P, TG])
            rel_c = tmp("rel_c", [P, TG])
            picked = tmp("picked", [P, TG, P])
            s2_win = tmp("s2_win", [P, TG])
            s2_sum = tmp("s2_sum", [P, TG])
            score = tmp("score", [P, TG])
            lscore = tmp("lscore", [P, RING, TG])
            top_col = tmp("top_col", [P, RING])
            run_max = tmp("run_max", [P, 1])
            grp_max = tmp("grp_max", [1, RING])
            grp_ref = tmp("grp_ref", [P, RING])
            neg_ref = tmp("neg_ref", [P, RING])
            expo = tmp("expo", [P, RING, TG])
            onehot = tmp("onehot", [P, 2, TG, P])
            below = tmp("below", [P, P])
            above = tmp("above", [P, P])
            keep = tmp("keep", [P, P])
            take = tmp("take", [P, P])
            part = tmp("part", [P, 2, P])
            all_max = tmp("all_max", [1, 1])

            idx_done = sem("idx_done")
            rows_here = sems("rows_here", RING)
            scat_done = sem("scat_done")
            onehot_made = sem("onehot_made")
            upd_done = sem("upd_done")
            init_done = sem("init_done")
            rel_done = sem("rel_done")
            s2_part = sem("s2_part")
            s2_set = sem("s2_set")
            s2_add = sem("s2_add")
            sc_done = sem("sc_done")
            ls_done = sem("ls_done")
            top_done = sem("top_done")
            run_done = sem("run_done")
            turn_done = sem("turn_done")
            max_done = sem("max_done")
            bc_done = sem("bc_done")
            ref_done = sem("ref_done")
            neg_done = sem("neg_done")
            exp_done = sem("exp2_done")
            relc_done = sem("relc_done")
            ref_moved = sem("ref_moved")
            factors = sem("factors")
            part_done = sem("part_done")
            kept = sem("kept")
            acc_done = sem("acc_done")
            fin = sem("fin")

            FULL = NG // RING
            block = att.enter_context(nc.Block())

            def walk(eng, step, lag):
                def at(i, u, known):
                    for k in lag:
                        v, t = (u - k) % RING, (u - k) // RING
                        if known is None or 0 <= (known * RING + u - k) < NG:
                            step(i + t, v, k)
                for u in range(RING):
                    at(0, u, 0)
                with eng.Fori(1, FULL) as i:
                    for u in range(RING):
                        at(i, u, None)
                for s in range(FULL * RING, NG + max(lag)):
                    at(FULL, s - FULL * RING, FULL)

            @block.gpsimd
            def _(pool):
                n_win = value(pool, ctrl[0:1, NG:NG + 1], NB, 1)

                def gather(i, u, k):
                    pool.wait_ge(idx_done, i * RING + u + 1)
                    if not isinstance(i, int) or i:
                        pool.wait_ge(scat_done, ((i - 1) * RING + u + 1) * n_win)
                    stand_alone(pool)
                    for q in range(TG):
                        pool.indirect_dma_start(rows_in[:, u, q, :], None, msg_table,
                                                bass.IndirectOffsetOnAxis(src_idx[:, u, q:q + 1], 0)
                                                ).then_inc(rows_here[u], 16)

                walk(pool, gather, (0,))

            @block.vector
            def _(dve):
                n_win = value(dve, ctrl[0:1, NG:NG + 1], NB, 1)

                def first_node(i, u):
                    stand_alone(dve)
                    return value(dve, ctrl[0:1, bass.ds(i * RING + u, 1)], NP - P)

                def index(i, u):
                    need(dve, rows_here[u], i * (16 * TG))
                    nc.vector.tensor_copy(src_idx[:, u, :], src_col[:, bass.ds((i * RING + u) * TG, TG)]
                                          ).then_inc(idx_done, 1)

                def scores(i, u):
                    g = i * RING + u
                    nc.vector.tensor_copy(s2_sum[:], pad_low[:, bass.ds(g * TG, TG)]).then_inc(s2_set, 1)
                    dve.wait_ge(s2_set, g + 1)
                    first = first_node(i, u)
                    with dve.Fori(0, n_win) as w:
                        n = g * n_win + w + 1
                        nc.vector.tensor_scalar(rel_a[:], dst_f[:, bass.ds(g * TG, TG)], base_b[:, bass.ds(g, 1)],
                                                win_off[:, bass.ds(w, 1)], ALU.subtract,
                                                ALU.subtract).then_inc(rel_done, 1)
                        dve.wait_ge(rel_done, n)
                        for q in range(TG):
                            ins = nc.vector.scalar_tensor_tensor(picked[:, q, :], iota_f[:], rel_a[:, q:q + 1],
                                                                 s2_b[:, window(first, w)], ALU.is_equal,
                                                                 ALU.mult, accum_out=s2_win[:, q:q + 1])
                        ins.then_inc(s2_part, 1)
                        dve.wait_ge(s2_part, n)
                        nc.vector.tensor_tensor(s2_sum[:], s2_sum[:], s2_win[:], ALU.add).then_inc(s2_add, 1)
                        dve.wait_ge(s2_add, n)
                        stand_alone(dve)
                    dve.wait_ge(rows_here[u], (i + 1) * (16 * TG))
                    nc.vector.tensor_tensor(score[:], s2_sum[:], rows_in[:, u, :, D], ALU.add).then_inc(sc_done, 1)
                    dve.wait_ge(sc_done, g + 1)
                    if not isinstance(i, int) or i:
                        dve.wait_ge(exp_done, g + 1 - RING)
                    nc.vector.scalar_tensor_tensor(lscore[:, u, :], score[:], SLOPE, score[:], ALU.mult,
                                                   ALU.max).then_inc(ls_done, 1)
                    dve.wait_ge(ls_done, g + 1)
                    if not isinstance(i, int) or i:
                        dve.wait_ge(turn_done, g + 1 - RING)
                    nc.vector.tensor_reduce(top_col[:, u:u + 1], lscore[:, u, :], AX, ALU.max).then_inc(top_done, 1)
                    dve.wait_ge(top_done, g + 1)
                    dve.wait_ge(run_done, g + 1)
                    nc.vector.tensor_tensor(run_max[:], run_max[:], top_col[:, u:u + 1], ALU.max).then_inc(run_done, 1)

                def group_max(i, u):
                    dve.wait_ge(turn_done, i * RING + u + 1)
                    nc.vector.tensor_reduce(grp_max[:, u:u + 1], ps_v[0:1, u % 2, 0:P], AX, ALU.max
                                            ).then_inc(max_done, 1)

                def make_onehots(i, u, w):
                    g = i * RING + u
                    n = g * n_win + w + 1
                    nc.vector.tensor_scalar(rel_c[:], dst_f[:, bass.ds(g * TG, TG)], base_b[:, bass.ds(g, 1)],
                                            win_off[:, bass.ds(w, 1)], ALU.subtract, ALU.subtract
                                            ).then_inc(relc_done, 1)
                    dve.wait_ge(relc_done, n)
                    for q in range(TG):
                        ins = nc.vector.tensor_scalar(onehot[:, u % 2, q, :], iota_f[:], rel_c[:, q:q + 1],
                                                      expo[:, u, q:q + 1], ALU.is_equal, ALU.mult)
                    ins.then_inc(onehot_made, 1)

                def move_ref(i, u, w, first):
                    n = (i * RING + u) * n_win + w + 1
                    r = ref[:, window(first, w)]
                    mine = grp_ref[:, u:u + 1]
                    nc.vector.tensor_scalar(below[:], r, mine, 0.0, ALU.subtract, ALU.min)
                    nc.vector.tensor_scalar(above[:], r, mine, 0.0, ALU.subtract, ALU.max)
                    nc.vector.tensor_scalar(r, r, mine, None, ALU.max).then_inc(ref_moved, 1)
                    dve.wait_ge(ref_moved, n)
                    stand_alone(dve)

                def update(i, u, w, first):
                    n = (i * RING + u) * n_win + w + 1
                    dve.wait_ge(scat_done, n)
                    dve.wait_ge(factors, 2 * n)
                    both = acc[:, :, window(first, w)]
                    nc.vector.tensor_tensor(part[:, :, :], ps_d[:, u % 2, 0:2 * P].rearrange("p (k n) -> p k n", k=2),
                                            take[:].unsqueeze(1).to_broadcast([P, 2, P]),
                                            ALU.mult).then_inc(part_done, 1)
                    nc.vector.tensor_tensor(both, both, keep[:].unsqueeze(1).to_broadcast([P, 2, P]),
                                            ALU.mult).then_inc(kept, 1)
                    dve.wait_ge(part_done, n)
                    dve.wait_ge(kept, n)
                    nc.vector.tensor_tensor(both, both, part[:, :, :], ALU.add).then_inc(upd_done, 1)
                    dve.wait_ge(upd_done, n + 1)
                    stand_alone(dve)

                def sums(i, u, after_none=False):
                    g = i * RING + u
                    dve.wait_ge(exp_done, g + 1)
                    if not isinstance(g, int) or g >= 2:
                        dve.wait_ge(scat_done, (g - 1) * n_win)
                    make_onehots(i, u, 0)
                    if not after_none:
                        pi, pu = (i, u - 1) if u else (i - 1, RING - 1)
                        update(pi, pu, n_win - 1, first_node(pi, pu))
                    first = first_node(i, u)
                    dve.wait_ge(ref_done, g + 1)
                    move_ref(i, u, 0, first)
                    with dve.If(n_win > 1):
                        with dve.Fori(1, n_win) as w:
                            dve.wait_ge(scat_done, g * n_win + w)
                            make_onehots(i, u, w)
                            update(i, u, w - 1, first)
                            move_ref(i, u, w, first)

                dve.sem_inc(upd_done, 1)
                nc.vector.memset(run_max[:], LOW).then_inc(run_done, 1)
                for u in range(RING):
                    index(0, u)

                def step(i, u, k):
                    if k == 0:
                        scores(i, u)
                        if not isinstance(i, int) or (i + 1) * RING + u < NG:
                            index(i + 1, u)
                    elif k == 1:
                        group_max(i, u)
                    else:
                        sums(i, u, after_none=isinstance(i, int) and i * RING + u == 0)

                walk(dve, step, (1, 0, 2))
                li, lu = (NG - 1) // RING, (NG - 1) % RING
                update(li, lu, n_win - 1, first_node(li, lu))
                dve.wait_ge(fin, 1)
                nc.vector.tensor_reduce(all_max[:], ps_wh[0:1, 0, 0, 0:P], AX, ALU.max).then_inc(fin, 1)
                dve.wait_ge(fin, 3)
                nc.vector.tensor_copy(final_max[:], ps_wh[:, 0, 1, 0:1])

            @block.tensor
            def _(pe):
                n_win = value(pe, ctrl[0:1, NG:NG + 1], NB, 1)

                def two_ago(s, g):
                    if not isinstance(g, int) or g >= 2:
                        pe.wait_ge(s, g - 1)

                def step(i, u, k):
                    g = i * RING + u
                    if k == 0:
                        pe.wait_ge(top_done, g + 1)
                        two_ago(neg_done, g)
                        nc.tensor.matmul(ps_v[0:1, u % 2, 0:P], top_col[:, u:u + 1], ident[:], start=True,
                                         stop=True).then_inc(turn_done, 1)
                    elif k == 1:
                        pe.wait_ge(max_done, g + 1)
                        two_ago(neg_done, g)
                        nc.tensor.matmul(ps_v[:, u % 2, 256:257], ones_row[:, 0:P], grp_max[:, u:u + 1], start=True,
                                         stop=True).then_inc(bc_done, 1)
                    else:
                        with pe.Fori(0, n_win) as w:
                            pe.wait_ge(onehot_made, g * n_win + w + 1)
                            pe.wait_ge(upd_done, g * n_win + w + 1)
                            for q in range(TG):
                                nc.tensor.matmul(ps_d[:, u % 2, 0:P], rows_in[:, u, q, 0:D], onehot[:, u % 2, q, :],
                                                 start=q == 0, stop=q == TG - 1)
                            for q in range(TG):
                                mm = nc.tensor.matmul(ps_d[:, u % 2, P:2 * P], ones[:], onehot[:, u % 2, q, :],
                                                      start=q == 0, stop=q == TG - 1)
                            mm.then_inc(scat_done, 1)

                walk(pe, step, (1, 2, 0))
                pe.wait_ge(run_done, NG + 1)
                nc.tensor.matmul(ps_wh[0:1, 0, 0, 0:P], run_max[:], ident[:], start=True, stop=True).then_inc(fin, 1)
                pe.wait_ge(fin, 2)
                nc.tensor.matmul(ps_wh[:, 0, 1, 0:1], ones_row[:, 0:P], all_max[:], start=True,
                                 stop=True).then_inc(fin, 1)

            @block.scalar
            def _(act):
                n_win = value(act, ctrl[0:1, NG:NG + 1], NB, 1)

                def exps(i, u):
                    g = i * RING + u
                    act.wait_ge(bc_done, g + 1)
                    if not isinstance(i, int) or i:
                        act.wait_ge(upd_done, (g + 1 - RING) * n_win + 1)
                    nc.scalar.activation(grp_ref[:, u:u + 1], ps_v[:, u % 2, 256:257], ACT.Copy).then_inc(ref_done, 1)
                    nc.scalar.activation(neg_ref[:, u:u + 1], ps_v[:, u % 2, 256:257], ACT.Copy,
                                         scale=-1.0).then_inc(neg_done, 1)
                    act.wait_ge(neg_done, g + 1)
                    nc.scalar.activation(expo[:, u, :], lscore[:, u, :], ACT.Exp, bias=neg_ref[:, u:u + 1]
                                         ).then_inc(exp_done, 1)

                def step(i, u, k):
                    if k == 1:
                        exps(i, u)
                    else:
                        g = i * RING + u
                        with act.Fori(0, n_win) as w:
                            act.wait_ge(ref_moved, g * n_win + w + 1)
                            nc.scalar.activation(keep[:], below[:], ACT.Exp).then_inc(factors, 1)
                            nc.scalar.activation(take[:], above[:], ACT.Exp, scale=-1.0).then_inc(factors, 1)

                walk(act, step, (1, 2))

        with ExitStack() as last:
            def tmp(name, shape, dt=F32):
                return last.enter_context(nc.sbuf_tensor(name, shape, dt))

            away = tmp("away", [P, CN])
            guard = tmp("guard", [P, CN])
            denom = tmp("denom", [P, CN])
            inv = tmp("inv", [P, CN])
            neigh = tmp("neigh", [P, CN])
            prod = tmp("prod", [P, CN])
            total = tmp("total", [P, CN])
            sloped = tmp("sloped", [P, CN])
            steep = tmp("steep", [P, CN])
            y = tmp("y", [P, NB, D])
            st = tmp("st2", [P, CB, 6])
            mv = tmp("mv2", [P, CB, 2])

            away_done = sem("away_done")
            guard_done = sem("guard_done")
            den_done = sem("den_done")
            inv_done = sem("inv_done")
            neigh_done = sem("neigh_done")
            mix_done = sem("mix_done")
            y_mm = sem("y_mm")
            slope_done = sem("slope_done")
            steep_done = sem("steep_done")
            y_done = sem("y_done")
            stat_done = sem("stat2_done")
            aggr_done = sem("aggr2_done")
            var_done = sem("var2_done")
            std_done = sem("std2_done")
            rstd_done = sem("rstd2_done")
            norm_done = sem("norm_done")
            stored = sem("stored")

            block = last.enter_context(nc.Block())

            @block.vector
            def _(dve):
                for c in range(NC):
                    at = bass.ds(c * CN, CN)
                    need(dve, guard_done, c)
                    nc.vector.tensor_scalar(away[:], ref[:, at], final_max[:, 0:1], -FAR, ALU.subtract,
                                            ALU.max).then_inc(away_done, 1)
                    dve.wait_ge(guard_done, c + 1)
                    nc.vector.scalar_tensor_tensor(denom[:], guard[:], 1e-9, acc[:, 1, at], ALU.mult,
                                                   ALU.add).then_inc(den_done, 1)
                    dve.wait_ge(den_done, c + 1)
                    nc.vector.reciprocal(inv[:], denom[:]).then_inc(inv_done, 1)
                    dve.wait_ge(inv_done, c + 1)
                    nc.vector.tensor_tensor(neigh[:], acc[:, 0, at], inv[:], ALU.mult).then_inc(neigh_done, 1)
                    dve.wait_ge(neigh_done, c + 1)
                    need(dve, y_mm, c)
                    nc.vector.tensor_tensor(prod[:], neigh[:], x1_t[:, at], ALU.mult).then_inc(mix_done, 1)
                    nc.vector.tensor_tensor(total[:], neigh[:], x1_t[:, at], ALU.add).then_inc(mix_done, 1)
                    dve.wait_ge(slope_done, c + 1)
                    nc.vector.tensor_tensor(steep[:], ps_d_flat[:, 0:CN], sloped[:], ALU.max).then_inc(steep_done, 1)
                    dve.wait_ge(steep_done, c + 1)
                    ys = y[:, bass.ds(c * CB, CB), :]
                    nc.vector.tensor_tensor(ys, steep[:].rearrange("p (b d) -> p b d", d=D),
                                            x1[:, bass.ds(c * CB, CB), :], ALU.add).then_inc(y_done, 1)
                    dve.wait_ge(y_done, c + 1)
                    stats(dve, y, st, mv, c, stat_done, aggr_done).then_inc(var_done, 1)
                dve.wait_ge(std_done, 1)
                nc.vector.reciprocal(ln_rstd[:], ln_std[:]).then_inc(rstd_done, 1)
                dve.wait_ge(rstd_done, 1)
                for c in range(NC):
                    for b in range(CB):
                        k = bass.ds(c * CB + b, 1)
                        ys = y[:, k, :].rearrange("p a d -> p (a d)")
                        ins = nc.vector.tensor_scalar(ys, ys, ln_mean[:, k], ln_rstd[:, k], ALU.subtract, ALU.mult)
                    ins.then_inc(norm_done, 1)

            @block.scalar
            def _(act):
                for c in range(NC):
                    act.wait_ge(away_done, c + 1)
                    need(act, den_done, c)
                    nc.scalar.activation(guard[:], away[:], ACT.Exp, scale=-1.0).then_inc(guard_done, 1)
                    act.wait_ge(y_mm, c + 1)
                    need(act, steep_done, c)
                    nc.scalar.activation(sloped[:], ps_d_flat[:, 0:CN], ACT.Copy, scale=SLOPE).then_inc(slope_done, 1)
                act.wait_ge(var_done, NC)
                nc.scalar.activation(ln_std[:], ln_var[:], ACT.Sqrt).then_inc(std_done, 1)

            @block.tensor
            def _(pe):
                for c in range(NC):
                    pe.wait_ge(mix_done, (c + 1) * 2)
                    need(pe, steep_done, c)
                    for b in range(CB):
                        o = ps_d_flat[:, b * P:(b + 1) * P]
                        nc.tensor.matmul(o, prod[:, b * P:(b + 1) * P], w2[:], start=True, stop=False)
                        nc.tensor.matmul(o, total[:, b * P:(b + 1) * P], ident[:], start=False, stop=False)
                        mm = nc.tensor.matmul(o, ones_row[:, 0:P], b2[:], start=False, stop=True)
                    mm.then_inc(y_mm, 1)

            @block.sync
            def _(sp):
                whole = N // P
                for c in range(NC):
                    sp.wait_ge(norm_done, c + 1)
                    n = min(CB, whole - c * CB)
                    sp.dma_start(out[c * CN:c * CN + n * P, :].rearrange("(b p) d -> p b d", p=P),
                                 y[:, c * CB:c * CB + n, :]).then_inc(stored, 16)
                sp.dma_start(out[whole * P:N, :], y[0:N - whole * P, whole, :]).then_inc(stored, 16)
                sp.wait_ge(stored, (NC + 1) * 16)


def kernel(**inputs):
    import numpy as np
    import concourse.bacc as bacc
    from concourse.bass_utils import run_bass_kernel_spmd

    get = {k: np.asarray(v) for k, v in inputs.items()}
    pad = EP - E
    src = np.pad(get["src"], (0, pad))
    dst = np.pad(get["dst"], (0, pad), constant_values=PAD_DST)
    x = np.pad(get["x"], ((0, NP - N), (0, 0)))
    cols = lambda v: v.reshape(NT, P).T
    arrays = {
        "x_rows": x, "x_t": x.T,
        "f_t": np.pad(get["edge_attr_20"].T, ((0, 0), (0, pad))),
        "src_row": src, "dst_row": dst, "src_col": cols(src), "dst_col": cols(dst),
        "w_col": cols(np.pad(get["edge_weight"], (0, pad))),
        "watt_t": get["L1_gnn_Watt_w"].T, "att2": get["L1_gnn_a"].reshape(2, D).T,
    }
    for k in ("L0_gnn_W_in", "L0_gnn_b_in", "L0_gnn_Wf1", "L0_gnn_bf1", "L0_gnn_Wf2", "L0_gnn_bf2", "L0_gnn_Wo1",
              "L0_gnn_bo1", "L0_gnn_Wo2", "L0_gnn_bo2", "L1_gnn_W1_w", "L1_gnn_W1_b", "L1_gnn_W2_w", "L1_gnn_W2_b",
              "L1_gnn_Watt_b"):
        arrays[k] = get[k]
    arrays = {k: np.ascontiguousarray(v) for k, v in arrays.items()}
    nc = bacc.Bacc("TRN2", target_bir_lowering=False, num_devices=1)
    args = {k: nc.dram_tensor("in_" + k, v.shape, mybir.dt.from_np(v.dtype), kind="ExternalInput").ap()
            for k, v in arrays.items()}
    out = nc.dram_tensor("out", (N, D), F32, kind="ExternalOutput").ap()
    build(nc, args, out)
    return run_bass_kernel_spmd(nc, [{"in_" + k: v for k, v in arrays.items()}], core_ids=[0]).results[0]["out"]
```
